# Optimizing a Trainium2 kernel written in Bass

```python
import numpy as np
import jax
import jax.numpy as jnp

def _softmax(x, axis=-1):
    return jax.nn.softmax(x, axis=axis)

def _gelu(x):
    return jax.nn.gelu(x, approximate=True)

def _silu(x):
    return jax.nn.silu(x)

def _sigmoid(x):
    return jax.nn.sigmoid(x)

def _layernorm(x, axis=-1, eps=1e-05):
    m = jnp.mean(x, axis=axis, keepdims=True)
    v = jnp.var(x, axis=axis, keepdims=True)
    return (x - m) / jnp.sqrt(v + eps)

def _scatter_add(tgt, idx, src, axis=0):
    return tgt.at[idx].add(src)

def _segment_sum(src, seg, n):
    return jax.ops.segment_sum(src, seg, n)
kernel_name = 'mk_dlrm_tower_d1_rec_r8_1d9fb8'

def setup_inputs(seed: int=0):
    np.random.seed(seed)
    _w = jnp.asarray

    def _rec_inputs():
        import jax
        import jax.numpy as jnp
        _tk = jax.random.key(seed)
        ids = jnp.stack([jax.random.randint(jax.random.fold_in(_tk, 200 + f), (512,), 0, v, jnp.int32) for f, v in enumerate([125000, 1250, 12500, 1250, 12500, 1000, 1000, 12500, 12500, 1000, 1250, 1250, 12500, 1250, 1250, 1000, 1000, 12500, 1000, 1250, 1000, 1250, 12500, 1000, 12500, 1250])], axis=1)
        tbl_0 = 0.05 * jax.random.normal(jax.random.fold_in(_tk, 500 + 0), (125000, 128), jnp.float32)
        tbl_1 = 0.05 * jax.random.normal(jax.random.fold_in(_tk, 500 + 1), (1250, 128), jnp.float32)
        tbl_2 = 0.05 * jax.random.normal(jax.random.fold_in(_tk, 500 + 2), (12500, 128), jnp.float32)
        tbl_3 = 0.05 * jax.random.normal(jax.random.fold_in(_tk, 500 + 3), (1250, 128), jnp.float32)
        tbl_4 = 0.05 * jax.random.normal(jax.random.fold_in(_tk, 500 + 4), (12500, 128), jnp.float32)
        tbl_5 = 0.05 * jax.random.normal(jax.random.fold_in(_tk, 500 + 5), (1000, 128), jnp.float32)
        tbl_6 = 0.05 * jax.random.normal(jax.random.fold_in(_tk, 500 + 6), (1000, 128), jnp.float32)
        tbl_7 = 0.05 * jax.random.normal(jax.random.fold_in(_tk, 500 + 7), (12500, 128), jnp.float32)
        tbl_8 = 0.05 * jax.random.normal(jax.random.fold_in(_tk, 500 + 8), (12500, 128), jnp.float32)
        tbl_9 = 0.05 * jax.random.normal(jax.random.fold_in(_tk, 500 + 9), (1000, 128), jnp.float32)
        tbl_10 = 0.05 * jax.random.normal(jax.random.fold_in(_tk, 500 + 10), (1250, 128), jnp.float32)
        tbl_11 = 0.05 * jax.random.normal(jax.random.fold_in(_tk, 500 + 11), (1250, 128), jnp.float32)
        tbl_12 = 0.05 * jax.random.normal(jax.random.fold_in(_tk, 500 + 12), (12500, 128), jnp.float32)
        tbl_13 = 0.05 * jax.random.normal(jax.random.fold_in(_tk, 500 + 13), (1250, 128), jnp.float32)
        tbl_14 = 0.05 * jax.random.normal(jax.random.fold_in(_tk, 500 + 14), (1250, 128), jnp.float32)
        tbl_15 = 0.05 * jax.random.normal(jax.random.fold_in(_tk, 500 + 15), (1000, 128), jnp.float32)
        tbl_16 = 0.05 * jax.random.normal(jax.random.fold_in(_tk, 500 + 16), (1000, 128), jnp.float32)
        tbl_17 = 0.05 * jax.random.normal(jax.random.fold_in(_tk, 500 + 17), (12500, 128), jnp.float32)
        tbl_18 = 0.05 * jax.random.normal(jax.random.fold_in(_tk, 500 + 18), (1000, 128), jnp.float32)
        tbl_19 = 0.05 * jax.random.normal(jax.random.fold_in(_tk, 500 + 19), (1250, 128), jnp.float32)
        tbl_20 = 0.05 * jax.random.normal(jax.random.fold_in(_tk, 500 + 20), (1000, 128), jnp.float32)
        tbl_21 = 0.05 * jax.random.normal(jax.random.fold_in(_tk, 500 + 21), (1250, 128), jnp.float32)
        tbl_22 = 0.05 * jax.random.normal(jax.random.fold_in(_tk, 500 + 22), (12500, 128), jnp.float32)
        tbl_23 = 0.05 * jax.random.normal(jax.random.fold_in(_tk, 500 + 23), (1000, 128), jnp.float32)
        tbl_24 = 0.05 * jax.random.normal(jax.random.fold_in(_tk, 500 + 24), (12500, 128), jnp.float32)
        tbl_25 = 0.05 * jax.random.normal(jax.random.fold_in(_tk, 500 + 25), (1250, 128), jnp.float32)
        _rk = jax.random.fold_in(_tk, 7)
        r_dense_features = -0.000520686 + 1.00062 * jax.random.normal(jax.random.fold_in(_rk, 101), (512, 128), jnp.float32)
        W_top1 = 0.0405887 * jax.random.normal(jax.random.fold_in(_tk, 801), (607, 512), jnp.float32)
        W_top2 = 0.0441942 * jax.random.normal(jax.random.fold_in(_tk, 802), (512, 256), jnp.float32)
        W_top3 = 0.0625 * jax.random.normal(jax.random.fold_in(_tk, 803), (256, 1), jnp.float32)
        b_top1 = jnp.zeros((512,), jnp.float32)
        b_top2 = jnp.zeros((256,), jnp.float32)
        return (r_dense_features, ids, tbl_0, tbl_1, tbl_2, tbl_3, tbl_4, tbl_5, tbl_6, tbl_7, tbl_8, tbl_9, tbl_10, tbl_11, tbl_12, tbl_13, tbl_14, tbl_15, tbl_16, tbl_17, tbl_18, tbl_19, tbl_20, tbl_21, tbl_22, tbl_23, tbl_24, tbl_25, W_top1, b_top1, W_top2, b_top2, W_top3)
    r_dense_features, ids, tbl_0, tbl_1, tbl_2, tbl_3, tbl_4, tbl_5, tbl_6, tbl_7, tbl_8, tbl_9, tbl_10, tbl_11, tbl_12, tbl_13, tbl_14, tbl_15, tbl_16, tbl_17, tbl_18, tbl_19, tbl_20, tbl_21, tbl_22, tbl_23, tbl_24, tbl_25, W_top1, b_top1, W_top2, b_top2, W_top3 = _rec_inputs()

    def _L0_rec_setup():
        import jax, jax.numpy as jnp
        import numpy as np
        B, F, D = (2048, 26, 128)
        key = jax.random.key(seed)
        k1, k2 = jax.random.split(key)
        dense_features = jax.random.normal(k1, (B, D), dtype=jnp.float32)
        sparse_features = jax.random.normal(k2, (B, F, D), dtype=jnp.float32)
        return {'dense_features': dense_features, 'sparse_features': sparse_features}
    _L0_rec_all = _L0_rec_setup()
    _L0_rec_in = {k: v for k, v in _L0_rec_all.items() if k in ()}
    del _L0_rec_all
    return {'r_dense_features': r_dense_features, 'ids': ids, 'tbl_0': tbl_0, 'tbl_1': tbl_1, 'tbl_2': tbl_2, 'tbl_3': tbl_3, 'tbl_4': tbl_4, 'tbl_5': tbl_5, 'tbl_6': tbl_6, 'tbl_7': tbl_7, 'tbl_8': tbl_8, 'tbl_9': tbl_9, 'tbl_10': tbl_10, 'tbl_11': tbl_11, 'tbl_12': tbl_12, 'tbl_13': tbl_13, 'tbl_14': tbl_14, 'tbl_15': tbl_15, 'tbl_16': tbl_16, 'tbl_17': tbl_17, 'tbl_18': tbl_18, 'tbl_19': tbl_19, 'tbl_20': tbl_20, 'tbl_21': tbl_21, 'tbl_22': tbl_22, 'tbl_23': tbl_23, 'tbl_24': tbl_24, 'tbl_25': tbl_25, 'W_top1': W_top1, 'b_top1': b_top1, 'W_top2': W_top2, 'b_top2': b_top2, 'W_top3': W_top3}

def reference(r_dense_features, ids, tbl_0, tbl_1, tbl_2, tbl_3, tbl_4, tbl_5, tbl_6, tbl_7, tbl_8, tbl_9, tbl_10, tbl_11, tbl_12, tbl_13, tbl_14, tbl_15, tbl_16, tbl_17, tbl_18, tbl_19, tbl_20, tbl_21, tbl_22, tbl_23, tbl_24, tbl_25, W_top1, b_top1, W_top2, b_top2, W_top3):
    import jax
    import jax.numpy as jnp

    def _L0_rec_ref(dense_features, sparse_features):
        import jax, jax.numpy as jnp
        import numpy as np
        B, F, D = (2048, 26, 128)
        combined = jnp.concatenate([dense_features[:, None, :], sparse_features], axis=1)
        interactions = jnp.einsum('bfd,bgd->bfg', combined, combined)
        iu0, iu1 = np.triu_indices(F + 1, k=1)
        interactions_flat = interactions[:, iu0, iu1]
        return jnp.concatenate([dense_features, interactions_flat], axis=1)
    e = jnp.stack([tbl_0[ids[:, 0]], tbl_1[ids[:, 1]], tbl_2[ids[:, 2]], tbl_3[ids[:, 3]], tbl_4[ids[:, 4]], tbl_5[ids[:, 5]], tbl_6[ids[:, 6]], tbl_7[ids[:, 7]], tbl_8[ids[:, 8]], tbl_9[ids[:, 9]], tbl_10[ids[:, 10]], tbl_11[ids[:, 11]], tbl_12[ids[:, 12]], tbl_13[ids[:, 13]], tbl_14[ids[:, 14]], tbl_15[ids[:, 15]], tbl_16[ids[:, 16]], tbl_17[ids[:, 17]], tbl_18[ids[:, 18]], tbl_19[ids[:, 19]], tbl_20[ids[:, 20]], tbl_21[ids[:, 21]], tbl_22[ids[:, 22]], tbl_23[ids[:, 23]], tbl_24[ids[:, 24]], tbl_25[ids[:, 25]]], axis=1)
    z = _L0_rec_ref(r_dense_features, e)
    z = z.reshape(z.shape[0], -1)
    h = jnp.concatenate([z, r_dense_features], axis=1)
    h = jnp.maximum(h @ W_top1 + b_top1, 0.0)
    h = jnp.maximum(h @ W_top2 + b_top2, 0.0)
    y = h @ W_top3
    return y

_drawn_inputs = setup_inputs


def setup_inputs(seed=0):
    import zlib

    import numpy as np

    out = dict(_drawn_inputs(seed))
    spreads = {'b_top1': (0.0, 0.1), 'b_top2': (0.0, 0.1)}
    factors = {}
    for name, (base, spread) in spreads.items():
        noise = np.random.default_rng([zlib.crc32(name.encode()), seed]).standard_normal(out[name].shape)
        drawn = base * np.exp(spread * noise) if base else spread * noise
        out[name] = jnp.asarray(drawn.astype(out[name].dtype))
    for name, factor in factors.items():
        out[name] = (out[name] * factor).astype(out[name].dtype)
    return out
```

```python
import concourse.bass as bass
from concourse import mybir
from contextlib import ExitStack

F32 = mybir.dt.float32
I32 = mybir.dt.int32
ALU = mybir.AluOpType
ACT = mybir.ActivationFunctionType

P = 128
Q = 32
NQ = P // Q


def dlrm_tower(nc, dense, ids, tables, w1_pairs, w1_dense, w2, b2, w3, out):
    B, D = dense.shape
    NT = len(tables)
    NF = NT + 1
    TILES = B // P
    H1 = w1_dense.shape[2]
    H2 = w2.shape[1]
    PC = w1_pairs.shape[0] // P
    GQ = PC
    N1 = H1 // P
    N2 = H2 // P
    TG = 4
    GROUPS = [(a, min(a + TG, NT)) for a in range(0, NT, TG)]
    NG = len(GROUPS)
    GB = 4
    HALF = Q // 2
    HB = HALF // GB
    assert D == P and NF <= Q and GQ * NQ >= NF

    with ExitStack() as ctx:
        def sb(name, shape, dt=F32):
            return ctx.enter_context(nc.sbuf_tensor(name, shape, dt))

        def sem(name):
            return ctx.enter_context(nc.semaphore(name))

        ids_sb = sb("ids_sb", [P, TILES, NT], I32)
        dense_sb = sb("dense_sb", [P, TILES, D])
        rows = sb("rows", [P, TILES, NT, D])
        xt = sb("xt", [P, TILES, Q, NQ, Q])
        w1_sb = sb("w1_sb", [P, PC, H1])
        wd_parts = sb("wd_parts", [P, 2, H1])
        wd_sb = sb("wd_sb", [P, H1])
        w2_sb = sb("w2_sb", [P, N1, H2])
        b2_sb = sb("b2_sb", [P, N2])
        w3_sb = sb("w3_sb", [P, N2])
        ident = sb("ident", [P, P])
        gram = sb("gram", [P, 2, PC, P])
        h1 = sb("h1", [P, 2, N1, P])
        h2 = sb("h2", [P, 2, N2, P])
        y_sb = sb("y_sb", [1, B])

        ps_t = ctx.enter_context(nc.psum_tensor("ps_t", [P, 2, TG, P], F32))
        ps_g = ctx.enter_context(nc.psum_tensor("ps_g", [P, HB, 512], F32))
        ps_1 = ctx.enter_context(nc.psum_tensor("ps_1", [P, N1, P], F32))
        ps_2 = ctx.enter_context(nc.psum_tensor("ps_2", [P, N2 + 2, P], F32))

        ids_in = sem("ids_in")
        dense_in = sem("dense_in")
        wd_in = sem("wd_in")
        w1_in = sem("w1_in")
        w2_in = sem("w2_in")
        small_in = sem("small_in")
        gathered = [[sem(f"gathered_{t}_{g}") for g in range(NG)] for t in range(TILES)]
        zeroed = sem("zeroed")
        ident_ready = sem("ident_ready")
        pads_ready = sem("pads_ready")
        wd_ready = sem("wd_ready")
        transposed = sem("transposed")
        xt_ready = sem("xt_ready")
        gram_done = sem("gram_done")
        gram_dve = sem("gram_dve")
        gram_act = sem("gram_act")
        h1_done = sem("h1_done")
        h1_ready = sem("h1_ready")
        h2_done = sem("h2_done")
        h2_ready = sem("h2_ready")
        y_done = sem("y_done")
        y_ready = sem("y_ready")
        stored = sem("stored")

        block = ctx.enter_context(nc.Block())
        STEPS = 1 + TILES * NG

        @block.sync
        def _(sp):
            sp.dma_start(ids_sb[:], ids.rearrange("(t p) f -> p t f", p=P)).then_inc(ids_in, 16)
            sp.dma_start(dense_sb[:], dense.rearrange("(t p) d -> p t d", p=P)).then_inc(dense_in, 16)
            sp.dma_start(wd_parts[:], w1_dense.rearrange("a p n -> p a n")).then_inc(wd_in, 16)
            sp.dma_start(w1_sb[:], w1_pairs.rearrange("(c p) n -> p c n", p=P)).then_inc(w1_in, 16)
            sp.dma_start(w2_sb[:], w2.rearrange("(c p) n -> p c n", p=P)).then_inc(w2_in, 16)
            sp.dma_start(b2_sb[:], b2).then_inc(small_in, 16)
            sp.dma_start(w3_sb[:], w3).then_inc(small_in, 16)
            sp.wait_ge(y_ready, TILES)
            sp.dma_start(out.rearrange("b o -> o b"), y_sb[:]).then_inc(stored, 16)
            sp.wait_ge(stored, 16)

        @block.gpsimd
        def _(pool):
            pool.wait_ge(zeroed, 1)
            pool.affine_select(out=ident[:], in_=ident[:], compare_op=ALU.not_equal, fill=1.0, base=0,
                               pattern=[[-1, P]], channel_multiplier=1).then_inc(ident_ready, 1)
            pool.wait_ge(ids_in, 16)
            for t in range(TILES):
                for g, (a, b) in enumerate(GROUPS):
                    for f in range(a, b):
                        pool.indirect_dma_start(
                            out=rows[:, t, f, :], out_offset=None, in_=tables[f],
                            in_offset=bass.IndirectOffsetOnAxis(ap=ids_sb[:, t, f:f + 1], axis=0),
                        ).then_inc(gathered[t][g], 16)

        def spread(eng, copy, t, half, j, sem_, waits):
            for q in range(NQ):
                n = min(GQ, NF - q * GQ)
                src = ps_g[Q * j:Q * j + NF, :, 0:GB * NQ * NF].rearrange("p k (s c) -> p c k s", s=GB)
                src = src[:, NF * j + GQ * q:NF * j + GQ * q + n]
                dst = gram[Q * q:Q * q + NF, t % 2, 0:n, Q * j + HALF * half:Q * j + HALF * half + HALF]
                last = copy(dst.rearrange("p c (k s) -> p c k s", s=GB), src)
            last.then_inc(sem_, 1)

        @block.vector
        def _(dve):
            dve.memset(ident[:], 0.0).then_inc(zeroed, 1)
            dve.memset(xt[:].rearrange("p t s j f -> p (t s j) f")[:, :, NF:Q], 0.0)
            dve.memset(gram[:], 1.0).then_inc(pads_ready, 1)
            dve.wait_ge(wd_in, 16)
            dve.tensor_tensor(wd_sb[:], wd_parts[:, 0], wd_parts[:, 1], ALU.add).then_inc(wd_ready, 1)

            dve.wait_ge(transposed, 1)
            for t in range(TILES):
                last = dve.tensor_copy(xt[:, t, :, :, 0].rearrange("p s j -> p j s"),
                                       ps_t[:, 0, t].rearrange("p (j s) -> p j s", j=NQ))
            last.then_inc(xt_ready, 1)

            def to_xt(t, g):
                step = 1 + t * NG + g
                a, b = GROUPS[g]
                dve.wait_ge(transposed, step + 1)
                dve.tensor_copy(xt[:, t, :, :, 1 + a:1 + b].rearrange("p s j f -> p f j s"),
                                ps_t[:, step % 2, 0:b - a].rearrange("p f (j s) -> p f j s", j=NQ)).then_inc(xt_ready, 1)

            for t in range(TILES):
                for g in range(NG):
                    to_xt(t, g)
                for half in range(2):
                    dve.wait_ge(gram_done, 2 * t + half + 1)
                    if t >= 2:
                        dve.wait_ge(h1_done, t - 1)
                    for j in (0, 1):
                        spread(dve, dve.tensor_copy, t, half, j, gram_dve, None)

        @block.scalar
        def _(act):
            act.wait_ge(small_in, 32)
            act.wait_ge(pads_ready, 1)

            def mlp(t):
                act.wait_ge(h1_done, t + 1)
                act.activation(h1[:, t % 2], ps_1[:], ACT.Relu).then_inc(h1_ready, 1)
                act.wait_ge(h2_done, t + 1)
                for m in range(N2):
                    last = act.activation(h2[:, t % 2, m], ps_2[:, m], ACT.Relu, bias=b2_sb[:, m:m + 1])
                last.then_inc(h2_ready, 1)
                act.wait_ge(y_done, t + 1)
                act.copy(y_sb[0:1, t * P:(t + 1) * P], ps_2[0:1, N2]).then_inc(y_ready, 1)

            for t in range(TILES):
                for half in range(2):
                    act.wait_ge(gram_done, 2 * t + half + 1)
                    if t >= 2:
                        act.wait_ge(h1_done, t - 1)
                    for j in (2, 3):
                        spread(act, act.copy, t, half, j, gram_act, None)
                    if half == 0 and t >= 1:
                        mlp(t - 1)
            mlp(TILES - 1)

        @block.tensor
        def _(pe):
            pe.wait_ge(ident_ready, 1)
            pe.wait_ge(dense_in, 16)
            for t in range(TILES):
                last = pe.transpose(ps_t[:, 0, t], dense_sb[:, t], ident[:])
            last.then_inc(transposed, 1)

            def turn(t):
                for g, (a, b) in enumerate(GROUPS):
                    step = 1 + t * NG + g
                    pe.wait_ge(gathered[t][g], 16 * (b - a))
                    if step >= 2:
                        pe.wait_ge(xt_ready, step - 1)
                    for f in range(a, b):
                        last = pe.transpose(ps_t[:, step % 2, f - a], rows[:, t, f], ident[:])
                    last.then_inc(transposed, 1)

            def products(t, half):
                pe.wait_ge(xt_ready, 1 + (t + 1) * NG)
                if t == 0 and half == 0:
                    pe.wait_ge(pads_ready, 1)
                before = 2 * t + half
                if before:
                    pe.wait_ge(gram_dve, 2 * before)
                    pe.wait_ge(gram_act, 2 * before)
                for i in range(HALF):
                    s = half * HALF + i
                    c = (i % GB) * NQ * NF
                    last = pe.matmul(ps_g[:, i // GB, c:c + NQ * NF], xt[:, t, s].rearrange("p j f -> p (j f)"), xt[:, t, s, :, 0:NF], start=True, stop=True)
                last.then_inc(gram_done, 1)

            def layer1(t):
                if t == 0:
                    pe.wait_ge(w1_in, 16)
                    pe.wait_ge(wd_ready, 1)
                pe.wait_ge(gram_dve, 4 * (t + 1))
                pe.wait_ge(gram_act, 4 * (t + 1))
                if t:
                    pe.wait_ge(h1_ready, t)
                for n in range(N1):
                    pe.matmul(ps_1[:, n], wd_sb[:, n * P:(n + 1) * P], xt[:, t, :, :, 0].rearrange("p s j -> p j s"),
                              start=True, stop=False)
                    for c in range(PC):
                        last = pe.matmul(ps_1[:, n], w1_sb[:, c, n * P:(n + 1) * P], gram[:, t % 2, c],
                                         start=False, stop=(c == PC - 1))
                last.then_inc(h1_done, 1)

            def layers23(t):
                if t == 0:
                    pe.wait_ge(w2_in, 16)
                    pe.wait_ge(small_in, 32)
                pe.wait_ge(h1_ready, t + 1)
                if t:
                    pe.wait_ge(y_ready, t)
                for m in range(N2):
                    for k in range(N1):
                        last = pe.matmul(ps_2[:, m], w2_sb[:, k, m * P:(m + 1) * P], h1[:, t % 2, k],
                                         start=(k == 0), stop=(k == N1 - 1))
                last.then_inc(h2_done, 1)
                pe.wait_ge(h2_ready, t + 1)
                for m in range(N2):
                    last = pe.matmul(ps_2[0:1, N2], w3_sb[:, m:m + 1], h2[:, t % 2, m],
                                     start=(m == 0), stop=(m == N2 - 1))
                last.then_inc(y_done, 1)

            for t in range(TILES):
                turn(t)
                products(t, 0)
                if t:
                    layer1(t - 1)
                products(t, 1)
                if t:
                    layers23(t - 1)
            layer1(TILES - 1)
            layers23(TILES - 1)


def kernel(**inputs):
    import numpy as np
    import concourse.bacc as bacc
    from concourse.bass_utils import run_bass_kernel_spmd

    nc = bacc.Bacc("TRN2", target_bir_lowering=False, num_devices=1)
    arrays = {}

    def dram(name, a):
        a = np.ascontiguousarray(a)
        arrays[name] = a
        return nc.dram_tensor(name, a.shape, mybir.dt.from_np(a.dtype), kind="ExternalInput").ap()

    dense = inputs["r_dense_features"]
    D = dense.shape[1]
    ids = inputs["ids"]
    nt = ids.shape[1]
    nf = nt + 1
    w1 = np.asarray(inputs["W_top1"])
    H1 = w1.shape[1]
    npairs = nf * (nf - 1) // 2
    gq = -(-nf // NQ)
    pairs = np.zeros((gq, NQ, Q, H1), w1.dtype)
    for g in range(1, nf):
        for f in range(g):
            pairs[g % gq, g // gq, f] = w1[D + f * (nf - 1) - f * (f - 1) // 2 + g - f - 1]
    pairs[0, 0, nf] = np.asarray(inputs["b_top1"])
    w1_dense = np.stack([w1[0:D], w1[D + npairs:]])
    args = [dram("dense", dense), dram("ids", ids),
            [dram(f"tbl_{i}", inputs[f"tbl_{i}"]) for i in range(nt)],
            dram("w1_pairs", pairs.reshape(gq * P, H1)), dram("w1_dense", w1_dense),
            dram("w2", inputs["W_top2"]),
            dram("b2", np.asarray(inputs["b_top2"]).reshape(-1, P).T),
            dram("w3", np.asarray(inputs["W_top3"]).reshape(-1, P).T)]
    out = nc.dram_tensor("y", (dense.shape[0], 1), F32, kind="ExternalOutput").ap()
    dlrm_tower(nc, *args, out)
    r = run_bass_kernel_spmd(nc, [arrays], core_ids=[0])
    return r.results[0]["y"]
```

```python
import concourse.bass as bass
from concourse import mybir
from contextlib import ExitStack

F32 = mybir.dt.float32
F32R = mybir.dt.float32r
I32 = mybir.dt.int32
ALU = mybir.AluOpType
ACT = mybir.ActivationFunctionType

P = 128
Q = 32
NQ = P // Q
KC = 8
NPICK = 7
RING = 8


def dlrm_tower(nc, dense, ids, picked_ids, tables, picked, w1_pairs, w1_dense, w2, b2, w3, out):
    B, D = dense.shape
    NT = len(tables)
    NP = len(picked)
    NF = 1 + NT + NP
    ROWS = picked[0].shape[0]
    KP = ROWS // KC
    SPLIT = KP - KP % 16
    TILES = B // P
    H1 = w1_dense.shape[2]
    H2 = w2.shape[1]
    PC = w1_pairs.shape[0] // P
    GQ = PC
    N1 = H1 // P
    N2 = H2 // P
    TG = 4
    GROUPS = [(a, min(a + TG, NT)) for a in range(0, NT, TG)]
    NG = len(GROUPS)
    GB = 4
    PARTS = 4
    PART = Q // PARTS
    PB = PART // GB
    assert D == P and NF <= Q and GQ * NQ >= NF

    with ExitStack() as ctx:
        def sb(name, shape, dt=F32):
            return ctx.enter_context(nc.sbuf_tensor(name, shape, dt))

        def sem(name):
            return ctx.enter_context(nc.semaphore(name))

        ids_sb = sb("ids_sb", [P, TILES, NT], I32)
        dense_sb = sb("dense_sb", [P, TILES, D])
        rows = sb("rows", [P, 2, NT, D])
        pick_ids = sb("pick_ids", [KP, NP, B], I32)
        row_no = sb("row_no", [KP, KC])
        table = sb("table", [KP, 2, KC, D])
        table_hi = sb("table_hi", [KP, 2, KC, D], F32R)
        table_lo = sb("table_lo", [KP, 2, KC, D], F32R)
        onehot = sb("onehot", [KP, RING, B], F32R)
        xt = sb("xt", [P, TILES, Q, NQ, Q])
        w1_sb = sb("w1_sb", [P, PC, H1])
        wd_parts = sb("wd_parts", [P, 2, H1])
        wd_sb = sb("wd_sb", [P, H1])
        w2_sb = sb("w2_sb", [P, N1, H2])
        b2_sb = sb("b2_sb", [P, N2])
        w3_sb = sb("w3_sb", [P, N2])
        ident = sb("ident", [P, P])
        gram = sb("gram", [P, 2, PC, P])
        h1 = sb("h1", [P, 2, N1, P])
        h2 = sb("h2", [P, 2, N2, P])
        y_sb = sb("y_sb", [1, B])

        ps_t = ctx.enter_context(nc.psum_tensor("ps_t", [P, 2, TG, P], F32))
        ps_g = ctx.enter_context(nc.psum_tensor("ps_g", [P, 2, PB, 512], F32))
        ps_1 = ctx.enter_context(nc.psum_tensor("ps_1", [P, N1, P], F32))
        ps_2 = ctx.enter_context(nc.psum_tensor("ps_2", [P, 4, P], F32))

        ids_in = sem("ids_in")
        dense_in = sem("dense_in")
        wd_in = sem("wd_in")
        w1_in = sem("w1_in")
        w2_in = sem("w2_in")
        small_in = sem("small_in")
        gathered = [[sem(f"gathered_{t}_{g}") for g in range(NG)] for t in range(TILES)]
        zeroed = sem("zeroed")
        ident_ready = sem("ident_ready")
        row_no_ready = sem("row_no_ready")
        table_in = [sem("table_in_even"), sem("table_in_odd")]
        hi_ready = sem("hi_ready")
        lo_ready = sem("lo_ready")
        onehot_ready = sem("onehot_ready")
        onehot_used = sem("onehot_used")
        picked_ready = sem("picked_ready")
        pads_ready = sem("pads_ready")
        wd_ready = sem("wd_ready")
        transposed = sem("transposed")
        xt_ready = sem("xt_ready")
        gram_done = sem("gram_done")
        gram_dve = sem("gram_dve")
        gram_act = sem("gram_act")
        h1_done = sem("h1_done")
        h1_ready = sem("h1_ready")
        h2_done = sem("h2_done")
        h2_ready = sem("h2_ready")
        y_done = sem("y_done")
        y_ready = sem("y_ready")
        stored = sem("stored")

        block = ctx.enter_context(nc.Block())
        PICK_SLOTS = list(range(1, NP))[:NG]

        @block.sync
        def _(sp):
            sp.dma_start(ids_sb[:], ids.rearrange("(t p) f -> p t f", p=P)).then_inc(ids_in, 16)

            def load_table(n):
                src = picked[n].rearrange("(p c) d -> p c d", c=KC)
                if n >= 2:
                    sp.wait_ge(hi_ready, n - 1)
                    sp.wait_ge(lo_ready, n - 1)
                for a, b in ((0, SPLIT), (SPLIT, KP)):
                    sp.dma_start(table[a:b, n % 2], src[a:b]).then_inc(table_in[n % 2], 16)
                    sp.dma_start(pick_ids[a:b, n], bass.AP(picked_ids.tensor, n * B, [[0, b - a], [1, B]]),
                                 ).then_inc(table_in[n % 2], 16)

            load_table(0)
            sp.dma_start(dense_sb[:], dense.rearrange("(t p) d -> p t d", p=P)).then_inc(dense_in, 16)
            load_table(1)
            load_table(2)
            sp.dma_start(wd_parts[:], w1_dense.rearrange("a p n -> p a n")).then_inc(wd_in, 16)
            sp.dma_start(w1_sb[:], w1_pairs.rearrange("(c p) n -> p c n", p=P)).then_inc(w1_in, 16)
            sp.dma_start(w2_sb[:], w2.rearrange("(c p) n -> p c n", p=P)).then_inc(w2_in, 16)
            sp.dma_start(b2_sb[:], b2).then_inc(small_in, 16)
            sp.dma_start(w3_sb[:], w3).then_inc(small_in, 16)
            for n in range(3, NP):
                load_table(n)
            sp.wait_ge(y_ready, TILES)
            sp.dma_start(out.rearrange("b o -> o b"), y_sb[:]).then_inc(stored, 16)
            sp.wait_ge(stored, 16)

        @block.gpsimd
        def _(pool):
            pool.iota(row_no[:], pattern=[[1, KC]], base=0, channel_multiplier=KC,
                      allow_small_or_imprecise_dtypes=True).then_inc(row_no_ready, 1)
            pool.wait_ge(zeroed, 1)
            pool.affine_select(out=ident[:], in_=ident[:], compare_op=ALU.not_equal, fill=1.0, base=0,
                               pattern=[[-1, P]], channel_multiplier=1).then_inc(ident_ready, 1)
            pool.wait_ge(ids_in, 16)
            for t in range(TILES):
                for g, (a, b) in enumerate(GROUPS):
                    if t >= 2:
                        pool.wait_ge(transposed, 1 + (t - 2) * NG + g + 1)
                    for f in range(a, b):
                        pool.indirect_dma_start(
                            out=rows[:, t % 2, f, :], out_offset=None, in_=tables[f],
                            in_offset=bass.IndirectOffsetOnAxis(ap=ids_sb[:, t, f:f + 1], axis=0),
                        ).then_inc(gathered[t][g], 16)

        def spread(copy, t, part, j, signal):
            s0 = Q * j + PART * part
            for q in range(NQ):
                n = min(GQ, NF - q * GQ)
                src = ps_g[Q * j:Q * j + NF, part % 2, :, 0:GB * NQ * NF].rearrange("p k (s c) -> p c k s", s=GB)
                src = src[:, NF * j + GQ * q:NF * j + GQ * q + n]
                dst = gram[Q * q:Q * q + NF, t % 2, 0:n, s0:s0 + PART].rearrange("p c (k s) -> p c k s", s=GB)
                last = copy(dst, src)
            last.then_inc(signal, 1)

        @block.vector
        def _(dve):
            dve.memset(ident[:], 0.0).then_inc(zeroed, 1)
            dve.memset(xt[:].rearrange("p t s j f -> p (t s j) f")[:, :, NF:Q], 0.0)
            dve.memset(gram[:], 1.0).then_inc(pads_ready, 1)

            def one_hots(n):
                for c in range(KC):
                    i = n * KC + c
                    if i >= RING:
                        dve.wait_ge(onehot_used, i - RING + 1)
                    dve.tensor_scalar(onehot[:, i % RING], pick_ids[:, n], row_no[:, c:c + 1], None,
                                      ALU.is_equal).then_inc(onehot_ready, 1)

            def table_rest(n):
                dve.wait_ge(hi_ready, n + 1)
                if n >= 2:
                    dve.wait_ge(onehot_used, (n - 1) * KC)
                dve.tensor_tensor(table_lo[:, n % 2], table[:, n % 2], table_hi[:, n % 2].bitcast(F32),
                                  ALU.subtract).then_inc(lo_ready, 1)

            dve.wait_ge(row_no_ready, 1)
            for n in range(NP):
                dve.wait_ge(table_in[n % 2], 64 * (n // 2 + 1))
                table_rest(n)
                one_hots(n)
            dve.wait_ge(wd_in, 16)
            dve.tensor_tensor(wd_sb[:], wd_parts[:, 0], wd_parts[:, 1], ALU.add).then_inc(wd_ready, 1)
            for t in range(TILES):
                for part in range(PARTS):
                    dve.wait_ge(gram_done, PARTS * t + part + 1)
                    if t >= 2 and part == 0:
                        dve.wait_ge(h1_done, t - 1)
                    for j in (0, 1):
                        spread(dve.tensor_copy, t, part, j, gram_dve)

        @block.scalar
        def _(act):
            def hi(n):
                act.wait_ge(table_in[n % 2], 64 * (n // 2 + 1))
                if n >= 2:
                    act.wait_ge(onehot_used, (n - 1) * KC)
                act.copy(table_hi[:, n % 2], table[:, n % 2]).then_inc(hi_ready, 1)

            def picked_to_xt(n):
                act.wait_ge(onehot_used, (n + 1) * KC)
                src = (ps_1 if n % 2 == 0 else ps_2)[:].rearrange("p t (j s) -> p t j s", j=NQ)
                act.copy(xt[:, :, :, :, 1 + NT + n].rearrange("p t s j -> p t j s"), src).then_inc(picked_ready, 1)

            def to_xt(t, g):
                step = 1 + t * NG + g
                a, b = GROUPS[g]
                act.wait_ge(transposed, step + 1)
                act.copy(xt[:, t, :, :, 1 + a:1 + b].rearrange("p s j f -> p f j s"),
                         ps_t[:, step % 2, 0:b - a].rearrange("p f (j s) -> p f j s", j=NQ)).then_inc(xt_ready, 1)

            def spread_part(t, part):
                act.wait_ge(gram_done, PARTS * t + part + 1)
                if t >= 2 and part == 0:
                    act.wait_ge(h1_done, t - 1)
                for j in (2, 3):
                    spread(act.copy, t, part, j, gram_act)

            def relu1(t):
                act.wait_ge(h1_done, t + 1)
                act.activation(h1[:, t % 2], ps_1[:], ACT.Relu).then_inc(h1_ready, 1)

            def relu2(t):
                act.wait_ge(h2_done, t + 1)
                for m in range(N2):
                    last = act.activation(h2[:, t % 2, m], ps_2[:, m], ACT.Relu, bias=b2_sb[:, m:m + 1])
                last.then_inc(h2_ready, 1)

            def keep_y(t):
                act.wait_ge(y_done, t + 1)
                act.copy(y_sb[0:1, t * P:(t + 1) * P], ps_2[0:1, N2]).then_inc(y_ready, 1)

            hi(0)
            for n in range(NP):
                if n + 1 < NP:
                    hi(n + 1)
                if n == 0:
                    act.wait_ge(transposed, 1)
                    for t in range(TILES):
                        last = act.copy(xt[:, t, :, :, 0].rearrange("p s j -> p j s"),
                                        ps_t[:, 0, t].rearrange("p (j s) -> p j s", j=NQ))
                    last.then_inc(xt_ready, 1)
                picked_to_xt(n)
                if n in PICK_SLOTS:
                    to_xt(0, PICK_SLOTS.index(n))
            for g in range(len(PICK_SLOTS), NG):
                to_xt(0, g)
            act.wait_ge(small_in, 32)
            for t in range(TILES):
                if t:
                    relu1(t - 1)
                spread_part(t, 0)
                spread_part(t, 1)
                if t:
                    relu2(t - 1)
                spread_part(t, 2)
                spread_part(t, 3)
                if t:
                    keep_y(t - 1)
                if t + 1 < TILES:
                    for g in range(NG):
                        to_xt(t + 1, g)
            relu1(TILES - 1)
            relu2(TILES - 1)
            keep_y(TILES - 1)

        @block.tensor
        def _(pe):
            pe.wait_ge(ident_ready, 1)
            pe.wait_ge(dense_in, 16)
            for t in range(TILES):
                last = pe.transpose(ps_t[:, 0, t], dense_sb[:, t], ident[:])
            last.then_inc(transposed, 1)

            def pick(n):
                ps = (ps_1 if n % 2 == 0 else ps_2)[:].rearrange("p k b -> p (k b)")
                pe.wait_ge(hi_ready, n + 1)
                pe.wait_ge(lo_ready, n + 1)
                if n >= 2:
                    pe.wait_ge(picked_ready, n - 1)
                for c in range(KC):
                    pe.wait_ge(onehot_ready, n * KC + c + 1)
                    pe.matmul(ps, table_hi[:, n % 2, c], onehot[:, (n * KC + c) % RING],
                              start=(c == 0), stop=False)
                    pe.matmul(ps, table_lo[:, n % 2, c], onehot[:, (n * KC + c) % RING],
                              start=False, stop=(c == KC - 1)).then_inc(onehot_used, 1)

            def turn(t, first, end):
                for g in range(first, end):
                    a, b = GROUPS[g]
                    step = 1 + t * NG + g
                    pe.wait_ge(gathered[t][g], 16 * (b - a))
                    if step >= 2:
                        pe.wait_ge(xt_ready, step - 1)
                    for f in range(a, b):
                        last = pe.transpose(ps_t[:, step % 2, f - a], rows[:, t % 2, f], ident[:])
                    last.then_inc(transposed, 1)

            def products(t, part):
                before = PARTS * t + part
                if part == 0:
                    pe.wait_ge(xt_ready, 1 + (t + 1) * NG)
                if before == 0:
                    pe.wait_ge(pads_ready, 1)
                    pe.wait_ge(picked_ready, NP)
                if before >= 2:
                    pe.wait_ge(gram_dve, 2 * (before - 1))
                    pe.wait_ge(gram_act, 2 * (before - 1))
                for i in range(PART):
                    s = part * PART + i
                    c = (i % GB) * NQ * NF
                    last = pe.matmul(ps_g[:, part % 2, i // GB, c:c + NQ * NF], xt[:, t, s].rearrange("p j f -> p (j f)"),
                                     xt[:, t, s, :, 0:NF], start=True, stop=True)
                last.then_inc(gram_done, 1)

            def layer1(t, first, end):
                if t == 0 and first == 0:
                    pe.wait_ge(w1_in, 16)
                    pe.wait_ge(wd_ready, 1)
                if first == 0:
                    pe.wait_ge(gram_dve, 2 * PARTS * (t + 1))
                    pe.wait_ge(gram_act, 2 * PARTS * (t + 1))
                    if t:
                        pe.wait_ge(h1_ready, t)
                for n in range(first, end):
                    pe.matmul(ps_1[:, n], wd_sb[:, n * P:(n + 1) * P], xt[:, t, :, :, 0].rearrange("p s j -> p j s"),
                              start=True, stop=False)
                    for c in range(PC):
                        last = pe.matmul(ps_1[:, n], w1_sb[:, c, n * P:(n + 1) * P], gram[:, t % 2, c],
                                         start=False, stop=(c == PC - 1))
                if end == N1:
                    last.then_inc(h1_done, 1)

            def layer2(t):
                if t == 0:
                    pe.wait_ge(w2_in, 16)
                    pe.wait_ge(small_in, 32)
                pe.wait_ge(h1_ready, t + 1)
                if t:
                    pe.wait_ge(y_ready, t)
                for m in range(N2):
                    for k in range(N1):
                        last = pe.matmul(ps_2[:, m], w2_sb[:, k, m * P:(m + 1) * P], h1[:, t % 2, k],
                                         start=(k == 0), stop=(k == N1 - 1))
                last.then_inc(h2_done, 1)

            def layer3(t):
                pe.wait_ge(h2_ready, t + 1)
                for m in range(N2):
                    last = pe.matmul(ps_2[0:1, N2], w3_sb[:, m:m + 1], h2[:, t % 2, m],
                                     start=(m == 0), stop=(m == N2 - 1))
                last.then_inc(y_done, 1)

            for n in range(NP):
                pick(n)
                if n in PICK_SLOTS:
                    turn(0, PICK_SLOTS.index(n), PICK_SLOTS.index(n) + 1)
            turn(0, len(PICK_SLOTS), NG)
            for t in range(TILES):
                more = t + 1 < TILES
                products(t, 0)
                products(t, 1)
                if t:
                    layer2(t - 1)
                products(t, 2)
                products(t, 3)
                if t:
                    layer3(t - 1)
                if more:
                    turn(t + 1, 0, 2)
                layer1(t, 0, 2)
                if more:
                    turn(t + 1, 2, 4)
                layer1(t, 2, 3)
                if more:
                    turn(t + 1, 4, NG)
                layer1(t, 3, N1)
            layer2(TILES - 1)
            layer3(TILES - 1)


def kernel(**inputs):
    import numpy as np
    import concourse.bacc as bacc
    from concourse.bass_utils import run_bass_kernel_spmd

    nc = bacc.Bacc("TRN2", target_bir_lowering=False, num_devices=1)
    arrays = {}

    def dram(name, a):
        a = np.ascontiguousarray(a)
        arrays[name] = a
        return nc.dram_tensor(name, a.shape, mybir.dt.from_np(a.dtype), kind="ExternalInput").ap()

    dense = inputs["r_dense_features"]
    D = dense.shape[1]
    ids = inputs["ids"]
    nf = ids.shape[1] + 1
    w1 = np.asarray(inputs["W_top1"])
    H1 = w1.shape[1]
    npairs = nf * (nf - 1) // 2
    gq = -(-nf // NQ)
    sizes = [inputs[f"tbl_{i}"].shape[0] for i in range(nf - 1)]
    small = [i for i in range(nf - 1) if sizes[i] == min(sizes)]
    picked = small[:NPICK]
    gathered = [i for i in range(nf - 1) if i not in picked]
    order = [0] + [1 + i for i in gathered + picked]
    pairs = np.zeros((gq, NQ, Q, H1), w1.dtype)
    for g in range(1, nf):
        for f in range(g):
            lo, hi = sorted((order[f], order[g]))
            pairs[g % gq, g // gq, f] = w1[D + lo * (nf - 1) - lo * (lo - 1) // 2 + hi - lo - 1]
    pairs[0, 0, nf] = np.asarray(inputs["b_top1"])
    w1_dense = np.stack([w1[0:D], w1[D + npairs:]])
    ids = np.asarray(ids)
    args = [dram("dense", dense), dram("ids", ids[:, gathered]), dram("picked_ids", ids[:, picked].T),
            [dram(f"tbl_{i}", inputs[f"tbl_{i}"]) for i in gathered],
            [dram(f"tbl_{i}", inputs[f"tbl_{i}"]) for i in picked],
            dram("w1_pairs", pairs.reshape(gq * P, H1)), dram("w1_dense", w1_dense),
            dram("w2", inputs["W_top2"]),
            dram("b2", np.asarray(inputs["b_top2"]).reshape(-1, P).T),
            dram("w3", np.asarray(inputs["W_top3"]).reshape(-1, P).T)]
    out = nc.dram_tensor("y", (dense.shape[0], 1), F32, kind="ExternalOutput").ap()
    dlrm_tower(nc, *args, out)
    r = run_bass_kernel_spmd(nc, [arrays], core_ids=[0])
    return r.results[0]["y"]
```

```python
import concourse.bass as bass
from concourse import mybir
from contextlib import ExitStack

F32 = mybir.dt.float32
F32R = mybir.dt.float32r
I32 = mybir.dt.int32
ALU = mybir.AluOpType
ACT = mybir.ActivationFunctionType

P = 128
Q = 32
NQ = P // Q
PAIR_CHUNKS = 4
NPICK = 8
RAW = 3
KC = 8
KA = 1
WARM = 14


def pair_layout(nf):
    first = nf - PAIR_CHUNKS * NQ
    moved = first - 1
    spare = Q - moved
    assert moved <= NQ * (PAIR_CHUNKS - 1) and first + NQ * (PAIR_CHUNKS - 1) - 1 <= spare and nf < Q
    return first, moved, spare


def moved_slot(m):
    return (m - 1) % (PAIR_CHUNKS - 1), (m - 1) // (PAIR_CHUNKS - 1)


def dlrm_tower(nc, dense, ids, picked_ids, tables, picked, w1_pairs, w1_dense, w2, b2, w3, out):
    B, D = dense.shape
    NT = len(tables)
    NP = len(picked)
    NF = 1 + NT + NP
    ROWS = picked[0].shape[0]
    KP = ROWS // KC
    KD = KC - KA
    SPLIT = KP - KP % 16
    TILES = B // P
    H1 = w1_dense.shape[2]
    H2 = w2.shape[1]
    PC = w1_pairs.shape[0] // P
    G0, MOVED, SPARE = pair_layout(NF)
    N1 = H1 // P
    N2 = H2 // P
    TG = 4
    GROUPS = [(a, min(a + TG, NT)) for a in range(0, NT, TG)]
    NG = len(GROUPS)
    GB = 4
    MG = P - (Q - NF + 1)
    PARTS = 4
    PART = Q // PARTS
    PB = PART // GB
    assert D == P and PC == PAIR_CHUNKS

    with ExitStack() as ctx:
        def sb(name, shape, dt=F32):
            return ctx.enter_context(nc.sbuf_tensor(name, shape, dt))

        def sem(name):
            return ctx.enter_context(nc.semaphore(name))

        ids_sb = sb("ids_sb", [P, TILES, NT], I32)
        dense_sb = sb("dense_sb", [P, TILES, D])
        rows = sb("rows", [P, 2, NT, D])
        pick_ids = sb("pick_ids", [KP, NP, B], I32)
        row_no = sb("row_no", [KP, KC])
        table = sb("table", [KP, RAW, KC, D])
        table_hi = sb("table_hi", [KP, 2, KC, D], F32R)
        table_lo = sb("table_lo", [KP, 2, KC, D], F32R)
        neg_row_no = sb("neg_row_no", [KP, KC])
        distance = sb("distance", [KP, B])
        onehot = sb("onehot", [KP, KD + 2 * KA, B], F32R)
        xt = sb("xt", [P, TILES, Q, NQ, Q])
        w1_sb = sb("w1_sb", [P, PC, H1])
        wd_parts = sb("wd_parts", [P, 2, H1])
        wd_sb = sb("wd_sb", [P, H1])
        w2_sb = sb("w2_sb", [P, N1, H2])
        b2_sb = sb("b2_sb", [P, N2])
        w3_sb = sb("w3_sb", [P, N2])
        ident = sb("ident", [P, P])
        gram = sb("gram", [P, 2, PC, P])
        side = sb("side", [MOVED, 2, MOVED, P])
        h1 = sb("h1", [P, 2, N1, P])
        h2 = sb("h2", [P, 2, N2, P])
        y_sb = sb("y_sb", [1, B])

        ps_t = ctx.enter_context(nc.psum_tensor("ps_t", [P, 2, TG, P], F32))
        ps_g = ctx.enter_context(nc.psum_tensor("ps_g", [P, 2, PB, 512], F32))
        ps_1 = ctx.enter_context(nc.psum_tensor("ps_1", [P, N1, P], F32))
        ps_2 = ctx.enter_context(nc.psum_tensor("ps_2", [P, 4, P], F32))

        ids_in = sem("ids_in")
        dense_in = sem("dense_in")
        wd_in = sem("wd_in")
        w1_in = sem("w1_in")
        w2_in = sem("w2_in")
        small_in = sem("small_in")
        gathered = [[sem(f"gathered_{t}_{g}") for g in range(NG)] for t in range(TILES)]
        zeroed = sem("zeroed")
        ident_ready = sem("ident_ready")
        row_no_ready = sem("row_no_ready")
        table_in = [sem(f"table_in_{i}") for i in range(RAW)]
        hi_ready = sem("hi_ready")
        lo_ready = sem("lo_ready")
        onehot_dve = sem("onehot_dve")
        distance_ready = sem("distance_ready")
        onehot_act = sem("onehot_act")
        onehot_used = sem("onehot_used")
        picked_ready = sem("picked_ready")
        pads_ready = sem("pads_ready")
        wd_ready = sem("wd_ready")
        transposed = sem("transposed")
        xt_ready = sem("xt_ready")
        gram_done = sem("gram_done")
        gram_dve = sem("gram_dve")
        gram_act = sem("gram_act")
        short_in = [sem("short_in_even"), sem("short_in_odd")]
        short_in_pool = sem("short_in_pool")
        h1_done = sem("h1_done")
        h1_ready = sem("h1_ready")
        h1_ready_dve = sem("h1_ready_dve")
        h2_done = sem("h2_done")
        h2_ready = sem("h2_ready")
        h2_ready_dve = sem("h2_ready_dve")
        y_done = sem("y_done")
        y_ready = sem("y_ready")
        stored = sem("stored")

        block = ctx.enter_context(nc.Block())
        MOVES = -(-MOVED // (PC - 1))
        POOL_MOVES = range(MOVES - 1, MOVES)
        SP_MOVES = [range(MOVES)] * (TILES - 1) + [range(MOVES - 1)]
        PICK_SLOTS = list(range(NP - 1))[-NG:]
        assert len(PICK_SLOTS) == NG

        def split_done(n):
            return n + 2

        def move_short(eng, t, quadrants, signal):
            eng.wait_ge(gram_dve, 2 * PARTS * (t + 1))
            eng.wait_ge(gram_act, 2 * PARTS * (t + 1))
            for q in quadrants:
                m = 1 + q * (PC - 1)
                n = min(PC - 1, MOVED + 1 - m)
                assert moved_slot(m) == (0, q)
                eng.dma_start(gram[Q * q + SPARE:Q * (q + 1), t % 2, 0:n],
                              side[:, t % 2, m - 1:m - 1 + n]).then_inc(signal, 16)

        @block.sync
        def _(sp):
            sp.dma_start(ids_sb[:], ids).then_inc(ids_in, 16)

            def load_table(n):
                src = picked[n].rearrange("(p c) d -> p c d", c=KC)
                if n >= RAW:
                    sp.wait_ge(hi_ready, split_done(n - RAW))
                    sp.wait_ge(lo_ready, split_done(n - RAW))
                for a, b in ((0, SPLIT), (SPLIT, KP)):
                    sp.dma_start(table[a:b, n % RAW], src[a:b]).then_inc(table_in[n % RAW], 16)
                    sp.dma_start(pick_ids[a:b, n], bass.AP(picked_ids.tensor, n * B, [[0, b - a], [1, B]])
                                 ).then_inc(table_in[n % RAW], 16)

            load_table(0)
            sp.dma_start(dense_sb[:], dense.rearrange("(t p) d -> p t d", p=P)).then_inc(dense_in, 16)
            for n in range(1, NP):
                load_table(n)
            sp.dma_start(wd_parts[:], w1_dense.rearrange("a p n -> p a n")).then_inc(wd_in, 16)
            sp.dma_start(w1_sb[:], w1_pairs.rearrange("(c p) n -> p c n", p=P)).then_inc(w1_in, 16)
            sp.dma_start(w2_sb[:], w2.rearrange("(c p) n -> p c n", p=P)).then_inc(w2_in, 16)
            sp.dma_start(b2_sb[:], b2).then_inc(small_in, 16)
            sp.dma_start(w3_sb[:], w3).then_inc(small_in, 16)
            for t in range(TILES):
                move_short(sp, t, SP_MOVES[t], short_in[t % 2])
            sp.wait_ge(y_ready, TILES)
            sp.dma_start(out.rearrange("b o -> o b"), y_sb[:]).then_inc(stored, 16)
            sp.wait_ge(stored, 16)

        @block.gpsimd
        def _(pool):
            pool.iota(row_no[:], pattern=[[1, KC]], base=0, channel_multiplier=KC,
                      allow_small_or_imprecise_dtypes=True).then_inc(row_no_ready, 1)
            pool.iota(neg_row_no[:], pattern=[[-1, KC]], base=0, channel_multiplier=-KC,
                      allow_small_or_imprecise_dtypes=True).then_inc(row_no_ready, 1)
            pool.wait_ge(zeroed, 1)
            pool.affine_select(out=ident[:], in_=ident[:], compare_op=ALU.not_equal, fill=1.0, base=0,
                               pattern=[[-1, P]], channel_multiplier=1).then_inc(ident_ready, 1)
            pool.wait_ge(ids_in, 16)
            for t in range(TILES):
                for g, (a, b) in enumerate(GROUPS):
                    if t >= 2:
                        pool.wait_ge(transposed, 1 + (t - 2) * NG + g + 1)
                    for f in range(a, b):
                        pool.indirect_dma_start(
                            out=rows[:, t % 2, f, :], out_offset=None, in_=tables[f],
                            in_offset=bass.IndirectOffsetOnAxis(ap=ids_sb[:, t, f:f + 1], axis=0),
                        ).then_inc(gathered[t][g], 16)
            move_short(pool, TILES - 1, POOL_MOVES, short_in_pool)

        def ps_h1(t, n):
            if t < TILES - 1:
                return ps_1[:, n]
            half, k = divmod(n, N1 // 2)
            return ps_g[:, 0, half, k * P:(k + 1) * P]

        def ps_h2(t, m):
            return ps_2[:, m] if t < TILES - 1 else ps_g[:, 1, m, 0:P]

        def act_slot(n, c):
            return KD + n % 2 * KA + c - KD

        def spread(copy, t, part, j, signal):
            s0 = Q * j + PART * part
            block_j = ps_g[Q * j:Q * j + NF - 1, part % 2, :, 0:GB * NQ * NF].rearrange("p k (s c) -> p c k s", s=GB)
            block_j = block_j[:, NF * j:NF * j + NF]
            for q in range(NQ):
                copy(gram[Q * q:Q * q + NF - 1, t % 2, :, s0:s0 + PART].rearrange("p c (k s) -> p c k s", s=GB),
                     block_j[0:NF - 1, G0 + q::NQ])
            last = copy(side[:, t % 2, :, s0:s0 + PART].rearrange("p c (k s) -> p c k s", s=GB),
                        block_j[0:MOVED, 1:1 + MOVED])
            last.then_inc(signal, 1)

        @block.vector
        def _(dve):
            dve.memset(ident[:], 0.0).then_inc(zeroed, 1)
            dve.memset(xt[:].rearrange("p t s j f -> p (t s j) f")[:, :, NF:Q], 0.0)
            dve.memset(gram[:], 1.0).then_inc(pads_ready, 1)

            def one_hots(n, first=0, end=KD):
                for c in range(first, end):
                    if n:
                        dve.wait_ge(onehot_used, (n - 1) * KC + c + 1)
                    dve.tensor_scalar(onehot[:, c], pick_ids[:, n], row_no[:, c:c + 1], None,
                                      ALU.is_equal).then_inc(onehot_dve, 1)

            def table_rest(n, first=0, end=KC):
                dve.wait_ge(hi_ready, split_done(n) - (end < KC))
                if n >= 2:
                    dve.wait_ge(onehot_used, (n - 1) * KC)
                dve.tensor_tensor(table_lo[:, n % 2, first:end], table[:, n % RAW, first:end],
                                  table_hi[:, n % 2, first:end].bitcast(F32), ALU.subtract).then_inc(lo_ready, 1)

            dve.wait_ge(row_no_ready, 2)
            for n in range(NP):
                dve.wait_ge(table_in[n % RAW], 64 * (n // RAW + 1))
                if n == 0:
                    one_hots(n, 0, KC // 2)
                    table_rest(n, 0, KC // 2)
                    one_hots(n, KC // 2)
                    table_rest(n, KC // 2, KC)
                else:
                    table_rest(n)
                    one_hots(n)
            dve.wait_ge(wd_in, 16)
            dve.tensor_tensor(wd_sb[:], wd_parts[:, 0], wd_parts[:, 1], ALU.add).then_inc(wd_ready, 1)
            for t in range(TILES):
                for part in range(PARTS):
                    dve.wait_ge(gram_done, PARTS * t + part + 1)
                    if t >= 2 and part == 0:
                        dve.wait_ge(h1_done, t - 1)
                    for j in (0, 1):
                        spread(dve.tensor_copy, t, part, j, gram_dve)
            dve.wait_ge(small_in, 32)
            dve.wait_ge(h1_done, TILES + 1)
            dve.tensor_scalar(h1[:, (TILES - 1) % 2, N1 // 2:N1].rearrange("p k b -> p (k b)"),
                              ps_g[:, 0, 1, 0:N1 // 2 * P], 0.0, None, ALU.max).then_inc(h1_ready_dve, 1)
            dve.wait_ge(h2_done, TILES + 1)
            dve.tensor_scalar(h2[:, (TILES - 1) % 2, 1], ps_h2(TILES - 1, 1), b2_sb[:, 1:2], 0.0,
                              ALU.add, ALU.max).then_inc(h2_ready_dve, 1)

        @block.scalar
        def _(act):
            def hi(n):
                act.wait_ge(table_in[n % RAW], 64 * (n // RAW + 1))
                if n >= 2:
                    act.wait_ge(onehot_used, (n - 1) * KC)
                for a, b in ((0, KC // 2), (KC // 2, KC)) if n == 0 else ((0, KC),):
                    act.copy(table_hi[:, n % 2, a:b], table[:, n % RAW, a:b]).then_inc(hi_ready, 1)
                if n == 0:
                    act.wait_ge(row_no_ready, 2)
                for c in range(KD, KC):
                    i = n * KA + c - KD
                    if i:
                        act.wait_ge(onehot_act, i)
                    act.activation(distance[:], pick_ids[:, n], ACT.Abs,
                                   bias=neg_row_no[:, c:c + 1]).then_inc(distance_ready, 1)
                    act.wait_ge(distance_ready, i + 1)
                    act.activation(onehot[:, act_slot(n, c)], distance[:], ACT.Relu, scale=-1.0,
                                   bias=1.0).then_inc(onehot_act, 1)

            def picked_to_xt(n):
                act.wait_ge(onehot_used, (n + 1) * KC)
                src = (ps_1 if n % 2 == 0 else ps_2)[:].rearrange("p t (j s) -> p t j s", j=NQ)
                for a, b in ((0, 1), (1, TILES)) if n == NP - 1 else ((0, TILES),):
                    act.copy(xt[:, a:b, :, :, 1 + NT + n].rearrange("p t s j -> p t j s"),
                             src[:, a:b]).then_inc(picked_ready, 1)

            def to_xt(t, g):
                step = 1 + t * NG + g
                a, b = GROUPS[g]
                act.wait_ge(transposed, step + 1)
                act.copy(xt[:, t, :, :, 1 + a:1 + b].rearrange("p s j f -> p f j s"),
                         ps_t[:, step % 2, 0:b - a].rearrange("p f (j s) -> p f j s", j=NQ)).then_inc(xt_ready, 1)

            def spread_part(t, part):
                act.wait_ge(gram_done, PARTS * t + part + 1)
                if t >= 2 and part == 0:
                    act.wait_ge(h1_done, t - 1)
                for j in (2, 3):
                    spread(act.copy, t, part, j, gram_act)

            def relu1(t):
                act.wait_ge(h1_done, t + 1)
                act.activation(h1[:, t % 2], ps_1[:], ACT.Relu).then_inc(h1_ready, 1)

            def relu2(t):
                act.wait_ge(h2_done, t + 1)
                for m in range(N2):
                    last = act.activation(h2[:, t % 2, m], ps_2[:, m], ACT.Relu, bias=b2_sb[:, m:m + 1])
                last.then_inc(h2_ready, 1)

            def keep_y(t):
                act.wait_ge(y_done, t + 1)
                act.copy(y_sb[0:1, t * P:(t + 1) * P], ps_2[0:1, N2]).then_inc(y_ready, 1)

            hi(0)
            for n in range(NP):
                if n + 1 < NP:
                    hi(n + 1)
                if n == 0:
                    act.wait_ge(transposed, 1)
                    for t in range(TILES):
                        last = act.copy(xt[:, t, :, :, 0].rearrange("p s j -> p j s"),
                                        ps_t[:, 0, t].rearrange("p (j s) -> p j s", j=NQ))
                    last.then_inc(xt_ready, 1)
                picked_to_xt(n)
                if n in PICK_SLOTS:
                    to_xt(0, PICK_SLOTS.index(n))
            act.wait_ge(small_in, 32)
            for t in range(TILES):
                last_tile = t == TILES - 1
                spread_part(t, 0)
                if t:
                    relu1(t - 1)
                spread_part(t, 1)
                if t and not last_tile:
                    relu2(t - 1)
                spread_part(t, 2)
                if not last_tile:
                    to_xt(t + 1, 0)
                spread_part(t, 3)
                if last_tile:
                    relu2(t - 1)
                    keep_y(t - 1)
                else:
                    to_xt(t + 1, 1)
                    to_xt(t + 1, 2)
                    if t:
                        keep_y(t - 1)
                    for g in range(3, NG):
                        to_xt(t + 1, g)
            act.wait_ge(h1_done, TILES)
            act.activation(h1[:, (TILES - 1) % 2, 0:N1 // 2].rearrange("p k b -> p (k b)"),
                           ps_g[:, 0, 0, 0:N1 // 2 * P], ACT.Relu).then_inc(h1_ready, 1)
            act.wait_ge(h2_done, TILES)
            act.activation(h2[:, (TILES - 1) % 2, 0], ps_h2(TILES - 1, 0), ACT.Relu,
                           bias=b2_sb[:, 0:1]).then_inc(h2_ready, 1)
            keep_y(TILES - 1)

        @block.tensor
        def _(pe):
            pe.wait_ge(ident_ready, 1)
            for i in range(WARM):
                pe.matmul(ps_g[:, 0, 0, 0:P], ident[:], ident[:], start=True, stop=True)
            pe.wait_ge(dense_in, 16)
            for t in range(TILES):
                last = pe.transpose(ps_t[:, 0, t], dense_sb[:, t], ident[:])
            last.then_inc(transposed, 1)

            def pick(n):
                ps = (ps_1 if n % 2 == 0 else ps_2)[:].rearrange("p k b -> p (k b)")
                if n:
                    pe.wait_ge(hi_ready, split_done(n))
                    pe.wait_ge(lo_ready, split_done(n))
                if n >= 2:
                    pe.wait_ge(picked_ready, n - 1)
                for c in range(KC):
                    if n == 0 and c % (KC // 2) == 0:
                        pe.wait_ge(hi_ready, 1 + c // (KC // 2))
                        pe.wait_ge(lo_ready, 1 + c // (KC // 2))
                    if c < KD:
                        pe.wait_ge(onehot_dve, n * KD + c + 1)
                        columns = onehot[:, c]
                    else:
                        pe.wait_ge(onehot_act, n * KA + c - KD + 1)
                        columns = onehot[:, act_slot(n, c)]
                    pe.matmul(ps, table_hi[:, n % 2, c], columns, start=(c == 0), stop=False)
                    pe.matmul(ps, table_lo[:, n % 2, c], columns, start=False,
                              stop=(c == KC - 1)).then_inc(onehot_used, 1)

            def turn(t, first, end):
                for g in range(first, end):
                    a, b = GROUPS[g]
                    step = 1 + t * NG + g
                    pe.wait_ge(gathered[t][g], 16 * (b - a))
                    if step >= 2:
                        pe.wait_ge(xt_ready, step - 1)
                    for f in range(a, b):
                        last = pe.transpose(ps_t[:, step % 2, f - a], rows[:, t % 2, f], ident[:])
                    last.then_inc(transposed, 1)

            def products(t, part):
                before = PARTS * t + part
                if part == 0:
                    pe.wait_ge(xt_ready, 1 + (t + 1) * NG)
                if before == 0:
                    pe.wait_ge(pads_ready, 1)
                    pe.wait_ge(picked_ready, NP)
                if before == PARTS:
                    pe.wait_ge(picked_ready, NP + 1)
                if before >= 2:
                    pe.wait_ge(gram_dve, 2 * (before - 1))
                    pe.wait_ge(gram_act, 2 * (before - 1))
                for i in range(PART):
                    s = part * PART + i
                    c = (i % GB) * NQ * NF
                    last = pe.matmul(ps_g[0:MG, part % 2, i // GB, c:c + NQ * NF],
                                     xt[:, t, s].rearrange("p j f -> p (j f)")[:, 0:MG], xt[:, t, s, :, 0:NF],
                                     start=True, stop=True)
                last.then_inc(gram_done, 1)

            def layer1(t, first, end):
                if t == 0 and first == 0:
                    pe.wait_ge(w1_in, 16)
                    pe.wait_ge(wd_ready, 1)
                if first == 0:
                    pe.wait_ge(gram_dve, 2 * PARTS * (t + 1))
                    pe.wait_ge(gram_act, 2 * PARTS * (t + 1))
                    if t:
                        pe.wait_ge(h1_ready, t)
                for i in range(first, end):
                    if i == 0:
                        w, x = wd_sb[:], xt[:, t, :, :, 0].rearrange("p s j -> p j s")
                    else:
                        c = (PC - 1, *range(PC - 1))[i - 1]
                        w, x = w1_sb[:, c], gram[:, t % 2, c]
                    if i == 2:
                        pe.wait_ge(short_in[t % 2], 16 * sum(len(SP_MOVES[u]) for u in range(t % 2, t + 1, 2)))
                        if t == TILES - 1:
                            pe.wait_ge(short_in_pool, 16 * len(POOL_MOVES))
                    for n in range(N1):
                        first_of_bank = n == 0 or t == TILES - 1 and n == N1 // 2
                        last = pe.matmul(ps_h1(t, n), w[:, n * P:(n + 1) * P], x, start=(i == 0 and first_of_bank),
                                         stop=(i == PC), skip_group_check=True)
                        if i == PC and (n == N1 - 1 or t == TILES - 1 and n == N1 // 2 - 1):
                            last.then_inc(h1_done, 1)

            def layer2(t):
                if t == 0:
                    pe.wait_ge(w2_in, 16)
                    pe.wait_ge(small_in, 32)
                pe.wait_ge(h1_ready, t + 1)
                if t and t < TILES - 1:
                    pe.wait_ge(y_ready, t)
                for m in range(N2):
                    for k in range(N1):
                        if t == TILES - 1 and m == 0 and k == N1 // 2:
                            pe.wait_ge(h1_ready_dve, 1)
                        last = pe.matmul(ps_h2(t, m), w2_sb[:, k, m * P:(m + 1) * P], h1[:, t % 2, k],
                                         start=(k == 0), stop=(k == N1 - 1))
                    if m == N2 - 1 or t == TILES - 1:
                        last.then_inc(h2_done, 1)

            def layer3(t):
                pe.wait_ge(h2_ready, t + 1)
                if t == TILES - 1:
                    pe.wait_ge(y_ready, t)
                for m in range(N2):
                    if t == TILES - 1 and m == 1:
                        pe.wait_ge(h2_ready_dve, 1)
                    last = pe.matmul(ps_2[0:1, N2], w3_sb[:, m:m + 1], h2[:, t % 2, m],
                                     start=(m == 0), stop=(m == N2 - 1))
                last.then_inc(y_done, 1)

            for n in range(NP):
                pick(n)
                if n in PICK_SLOTS:
                    turn(0, PICK_SLOTS.index(n), PICK_SLOTS.index(n) + 1)
            products(0, 0)
            for t in range(TILES):
                last_tile = t == TILES - 1
                if t:
                    layer1(t - 1, 2, PC + 1)
                products(t, 1)
                if t and not last_tile:
                    layer2(t - 1)
                products(t, 2)
                if not last_tile:
                    turn(t + 1, 0, 1)
                products(t, 3)
                if last_tile:
                    layer2(t - 1)
                    layer1(t, 0, 2)
                    layer3(t - 1)
                else:
                    turn(t + 1, 1, 3)
                    if t:
                        layer3(t - 1)
                    layer1(t, 0, 1)
                    turn(t + 1, 3, NG)
                    layer1(t, 1, 2)
                    products(t + 1, 0)
            t = TILES - 1
            layer1(t, 2, PC + 1)
            layer2(t)
            layer3(t)


def kernel(**inputs):
    import numpy as np
    import concourse.bacc as bacc
    from concourse.bass_utils import run_bass_kernel_spmd

    nc = bacc.Bacc("TRN2", target_bir_lowering=False, num_devices=1)
    arrays = {}

    def dram(name, a):
        a = np.ascontiguousarray(a)
        arrays[name] = a
        return nc.dram_tensor(name, a.shape, mybir.dt.from_np(a.dtype), kind="ExternalInput").ap()

    dense = inputs["r_dense_features"]
    D = dense.shape[1]
    ids = inputs["ids"]
    nf = ids.shape[1] + 1
    w1 = np.asarray(inputs["W_top1"])
    H1 = w1.shape[1]
    npairs = nf * (nf - 1) // 2
    sizes = [inputs[f"tbl_{i}"].shape[0] for i in range(nf - 1)]
    small = [i for i in range(nf - 1) if sizes[i] == min(sizes)]
    picked = small[:NPICK]
    gathered = [i for i in range(nf - 1) if i not in picked]
    order = [0] + [1 + i for i in gathered + picked]
    first, moved, spare = pair_layout(nf)
    pairs = np.zeros((PAIR_CHUNKS, NQ, Q, H1), w1.dtype)
    for g in range(1, nf):
        for f in range(g):
            lo, hi = sorted((order[f], order[g]))
            if g < first:
                slot = (*moved_slot(g), spare + f)
            else:
                slot = ((g - first) // NQ, (g - first) % NQ, f)
            pairs[slot] = w1[D + lo * (nf - 1) - lo * (lo - 1) // 2 + hi - lo - 1]
    pairs[PAIR_CHUNKS - 1, NQ - 1, nf] = np.asarray(inputs["b_top1"])
    w1_dense = np.stack([w1[0:D], w1[D + npairs:]])
    ids = np.asarray(ids)
    args = [dram("dense", dense), dram("ids", ids[:, gathered].reshape(-1, P, len(gathered)).transpose(1, 0, 2)),
            dram("picked_ids", ids[:, picked].T),
            [dram(f"tbl_{i}", inputs[f"tbl_{i}"]) for i in gathered],
            [dram(f"tbl_{i}", inputs[f"tbl_{i}"]) for i in picked],
            dram("w1_pairs", pairs.reshape(PAIR_CHUNKS * P, H1)), dram("w1_dense", w1_dense),
            dram("w2", inputs["W_top2"]),
            dram("b2", np.asarray(inputs["b_top2"]).reshape(-1, P).T),
            dram("w3", np.asarray(inputs["W_top3"]).reshape(-1, P).T)]
    out = nc.dram_tensor("y", (dense.shape[0], 1), F32, kind="ExternalOutput").ap()
    dlrm_tower(nc, *args, out)
    r = run_bass_kernel_spmd(nc, [arrays], core_ids=[0])
    return r.results[0]["y"]
```
